# Optimizing a Trainium2 kernel written in Bass

```python
import numpy as np
import jax
import jax.numpy as jnp

def _softmax(x, axis=-1):
    return jax.nn.softmax(x, axis=axis)

def _gelu(x):
    return jax.nn.gelu(x, approximate=True)

def _silu(x):
    return jax.nn.silu(x)

def _sigmoid(x):
    return jax.nn.sigmoid(x)

def _layernorm(x, axis=-1, eps=1e-05):
    m = jnp.mean(x, axis=axis, keepdims=True)
    v = jnp.var(x, axis=axis, keepdims=True)
    return (x - m) / jnp.sqrt(v + eps)

def _scatter_add(tgt, idx, src, axis=0):
    return tgt.at[idx].add(src)

def _segment_sum(src, seg, n):
    return jax.ops.segment_sum(src, seg, n)
kernel_name = 'mk_cond_seq_d4_seqx_r4_067a0b'

def setup_inputs(seed: int=0):
    np.random.seed(seed)
    _w = jnp.asarray

    def _rec_inputs():
        import jax
        import jax.numpy as jnp
        _rk = jax.random.key(seed)
        x = 1.648e-05 + 1 * jax.random.normal(jax.random.fold_in(_rk, 1), (2, 1024, 288), jnp.float32)
        _lenS = 1024 - jax.random.randint(jax.random.fold_in(_rk, 7), (2,), 0, max(1, 1024 // 4) + 1, jnp.int32)
        _lenS2 = 1024 - jax.random.randint(jax.random.fold_in(_rk, 8), (2,), 0, max(1, 1024 // 4) + 1, jnp.int32)
        cond_1152 = 0.00914911 + 1.00357 * jax.random.normal(jax.random.fold_in(_rk, 11), (2, 288), jnp.float32)
        return (x, cond_1152)
    x, cond_1152 = _rec_inputs()

    def _L0_cond_setup():
        import jax, jax.numpy as jnp
        import numpy as np
        B, L, C = (8, 256, 288)
        H = 16
        D = C // H
        FF = int(C * 4.0)
        EPS = 1e-06

        def _layernorm(x):
            mu = jnp.mean(x, axis=-1, keepdims=True)
            var = jnp.mean(jnp.square(x - mu), axis=-1, keepdims=True)
            return (x - mu) * jax.lax.rsqrt(var + EPS)

        def _modulate(x, shift, scale):
            return x * (1.0 + scale) + shift

        def _attention(h, W_qkv, b_qkv, W_proj, b_proj):
            b, l, c = h.shape
            qkv = h @ W_qkv + b_qkv
            qkv = qkv.reshape(b, l, 3, H, D)
            q, k, v = (qkv[:, :, 0], qkv[:, :, 1], qkv[:, :, 2])
            scale = D ** (-0.5)
            scores = jnp.einsum('blhd,bmhd->bhlm', q * scale, k)
            attn = jax.nn.softmax(scores, axis=-1)
            o = jnp.einsum('bhlm,bmhd->blhd', attn, v).reshape(b, l, c)
            return o @ W_proj + b_proj
        key = jax.random.key(seed)
        ks = jax.random.split(key, 12)
        s = 0.02
        return {'x': jax.random.normal(ks[0], (B, L, C), jnp.float32), 'c': jax.random.normal(ks[1], (B, 1, C), jnp.float32), 'W_qkv': jax.random.normal(ks[2], (C, 3 * C), jnp.float32) * s, 'b_qkv': jnp.zeros((3 * C,), jnp.float32), 'W_proj': jax.random.normal(ks[3], (C, C), jnp.float32) * s, 'b_proj': jnp.zeros((C,), jnp.float32), 'W_fc1': jax.random.normal(ks[4], (C, FF), jnp.float32) * s, 'b_fc1': jnp.zeros((FF,), jnp.float32), 'W_fc2': jax.random.normal(ks[5], (FF, C), jnp.float32) * s, 'b_fc2': jnp.zeros((C,), jnp.float32), 'W_ada': jax.random.normal(ks[6], (C, 6 * C), jnp.float32) * s, 'b_ada': jnp.zeros((6 * C,), jnp.float32)}
    _L0_cond_all = _L0_cond_setup()
    _L0_cond_in = {k: v for k, v in _L0_cond_all.items() if k in ('W_qkv', 'b_qkv', 'W_proj', 'b_proj', 'W_fc1', 'b_fc1', 'W_fc2', 'b_fc2', 'W_ada', 'b_ada')}
    del _L0_cond_all

    def _L1_cond_setup():
        import jax, jax.numpy as jnp
        import numpy as np
        B, S, D = (8, 256, 288)
        H = 16
        HD = D // H
        HID = int(D * 4.0)
        LN_EPS = 1e-05

        def layer_norm(x, w, b):
            m = jnp.mean(x, axis=-1, keepdims=True)
            v = jnp.mean(jnp.square(x - m), axis=-1, keepdims=True)
            return (x - m) * jax.lax.rsqrt(v + LN_EPS) * w + b

        def modulate(x, shift, scale):
            return x * (1.0 + scale[:, None, :]) + shift[:, None, :]

        def attention(x, wq, wk, wv, wo, wo_b):
            b, s, d = x.shape
            q = (x @ wq).reshape(b, s, H, HD).transpose(0, 2, 1, 3)
            k = (x @ wk).reshape(b, s, H, HD).transpose(0, 2, 1, 3)
            v = (x @ wv).reshape(b, s, H, HD).transpose(0, 2, 1, 3)
            scale = 1.0 / np.sqrt(HD).astype(np.float32)
            att = jnp.einsum('bhqd,bhkd->bhqk', q, k) * scale
            att = jax.nn.softmax(att, axis=-1)
            out = jnp.einsum('bhqk,bhkd->bhqd', att, v)
            out = out.transpose(0, 2, 1, 3).reshape(b, s, d)
            return out @ wo + wo_b
        key = jax.random.key(seed)
        ks = jax.random.split(key, 16)
        s = 0.02
        return {'x': jax.random.normal(ks[0], (B, S, D), jnp.float32), 'c': jax.random.normal(ks[1], (B, D), jnp.float32), 'ln1_w': jnp.ones((D,), jnp.float32), 'ln1_b': jnp.zeros((D,), jnp.float32), 'wq': jax.random.normal(ks[2], (D, D), jnp.float32) * s, 'wk': jax.random.normal(ks[3], (D, D), jnp.float32) * s, 'wv': jax.random.normal(ks[4], (D, D), jnp.float32) * s, 'wo': jax.random.normal(ks[5], (D, D), jnp.float32) * s, 'wo_b': jnp.zeros((D,), jnp.float32), 'ln2_w': jnp.ones((D,), jnp.float32), 'ln2_b': jnp.zeros((D,), jnp.float32), 'fc1_w': jax.random.normal(ks[6], (D, HID), jnp.float32) * s, 'fc1_b': jnp.zeros((HID,), jnp.float32), 'fc2_w': jax.random.normal(ks[7], (HID, D), jnp.float32) * s, 'fc2_b': jnp.zeros((D,), jnp.float32), 'ada_w': jax.random.normal(ks[8], (D, 6 * D), jnp.float32) * s, 'ada_b': jnp.zeros((6 * D,), jnp.float32)}
    _L1_cond_all = _L1_cond_setup()
    _L1_cond_in = {k: v for k, v in _L1_cond_all.items() if k in ('ln1_w', 'ln1_b', 'wq', 'wk', 'wv', 'wo', 'wo_b', 'ln2_w', 'ln2_b', 'fc1_w', 'fc1_b', 'fc2_w', 'fc2_b', 'ada_w', 'ada_b')}
    del _L1_cond_all

    def _L2_cond_setup():
        import jax, jax.numpy as jnp
        import numpy as np
        N, T, D, H = (32, 256, 288, 16)
        DH = D // H
        MLP = int(D * 4.0)
        EPS = 1e-06

        def _layernorm(x):
            m = jnp.mean(x, axis=-1, keepdims=True)
            v = jnp.var(x, axis=-1, keepdims=True)
            return (x - m) * jax.lax.rsqrt(v + EPS)

        def _modulate(x, shift, scale):
            return x * (1.0 + scale[:, None, :]) + shift[:, None, :]

        def _attention(x, qkv_w, qkv_b, proj_w, proj_b):
            n, t, d = x.shape
            scale = DH ** (-0.5)
            qkv = x @ qkv_w + qkv_b
            qkv = qkv.reshape(n, t, 3, H, DH)
            q, k, v = (qkv[:, :, 0], qkv[:, :, 1], qkv[:, :, 2])
            attn = jnp.einsum('nthd,ntkd->nthk', q * scale, k)
            attn = jax.nn.softmax(attn, axis=-1)
            out = jnp.einsum('nthk,ntkd->nthd', attn, v)
            out = out.transpose(0, 2, 1, 3).reshape(n, t, d)
            return out @ proj_w + proj_b

        def _mlp(x, fc1_w, fc1_b, fc2_w, fc2_b):
            h = jax.nn.gelu(x @ fc1_w + fc1_b, approximate=False)
            return h @ fc2_w + fc2_b
        key = jax.random.key(seed)
        ks = jax.random.split(key, 14)
        s = 0.02
        return {'x': jax.random.normal(ks[0], (N, T, D), jnp.float32), 'c': jax.random.normal(ks[1], (N, D), jnp.float32), 'qkv_w': jax.random.normal(ks[2], (D, 3 * D), jnp.float32) * s, 'qkv_b': jax.random.normal(ks[3], (3 * D,), jnp.float32) * s, 'proj_w': jax.random.normal(ks[4], (D, D), jnp.float32) * s, 'proj_b': jax.random.normal(ks[5], (D,), jnp.float32) * s, 'fc1_w': jax.random.normal(ks[6], (D, MLP), jnp.float32) * s, 'fc1_b': jax.random.normal(ks[7], (MLP,), jnp.float32) * s, 'fc2_w': jax.random.normal(ks[8], (MLP, D), jnp.float32) * s, 'fc2_b': jax.random.normal(ks[9], (D,), jnp.float32) * s, 'ada_w': jax.random.normal(ks[10], (D, 6 * D), jnp.float32) * s, 'ada_b': jax.random.normal(ks[11], (6 * D,), jnp.float32) * s}
    _L2_cond_all = _L2_cond_setup()
    _L2_cond_in = {k: v for k, v in _L2_cond_all.items() if k in ('qkv_w', 'qkv_b', 'proj_w', 'proj_b', 'fc1_w', 'fc1_b', 'fc2_w', 'fc2_b', 'ada_w', 'ada_b')}
    del _L2_cond_all

    def _L3_cond_setup():
        import math
        import jax, jax.numpy as jnp
        import numpy as np
        B, T, D = (8, 256, 288)
        H = 16
        E = 4
        EPS = 1e-06

        def _layer_norm(x):
            mu = jnp.mean(x, axis=-1, keepdims=True)
            var = jnp.mean(jnp.square(x - mu), axis=-1, keepdims=True)
            return (x - mu) * jax.lax.rsqrt(var + EPS)

        def _modulate(x, shift, scale):
            return x * (1.0 + scale) + shift

        def _attention(y, qkv_w, qkv_b, out_w, out_b):
            b, t, d = y.shape
            hd = d // H
            qkv = y @ qkv_w + qkv_b
            q, k, v = jnp.split(qkv, 3, axis=-1)
            q = q.reshape(b, t, H, hd).transpose(0, 2, 1, 3)
            k = k.reshape(b, t, H, hd).transpose(0, 2, 1, 3)
            v = v.reshape(b, t, H, hd).transpose(0, 2, 1, 3)
            scores = jnp.einsum('bhqd,bhkd->bhqk', q, k) / math.sqrt(hd)
            attn = jax.nn.softmax(scores, axis=-1)
            out = jnp.einsum('bhqk,bhkd->bhqd', attn, v)
            out = out.transpose(0, 2, 1, 3).reshape(b, t, d)
            return out @ out_w + out_b
        key = jax.random.key(seed)
        ks = jax.random.split(key, 12)
        std = 0.02
        return {'x': jax.random.normal(ks[0], (B, T, D), dtype=jnp.float32), 'c': jax.random.normal(ks[1], (B, D), dtype=jnp.float32), 'qkv_w': jax.random.normal(ks[2], (D, 3 * D), dtype=jnp.float32) * std, 'qkv_b': jnp.zeros((3 * D,), dtype=jnp.float32), 'out_w': jax.random.normal(ks[3], (D, D), dtype=jnp.float32) * std, 'out_b': jnp.zeros((D,), dtype=jnp.float32), 'w1': jax.random.normal(ks[4], (D, E * D), dtype=jnp.float32) * std, 'b1': jnp.zeros((E * D,), dtype=jnp.float32), 'w2': jax.random.normal(ks[5], (E * D, D), dtype=jnp.float32) * std, 'b2': jnp.zeros((D,), dtype=jnp.float32), 'ada_w': jax.random.normal(ks[6], (D, 6 * D), dtype=jnp.float32) * std, 'ada_b': jnp.zeros((6 * D,), dtype=jnp.float32)}
    _L3_cond_all = _L3_cond_setup()
    _L3_cond_in = {k: v for k, v in _L3_cond_all.items() if k in ('qkv_w', 'qkv_b', 'out_w', 'out_b', 'w1', 'b1', 'w2', 'b2', 'ada_w', 'ada_b')}
    del _L3_cond_all
    return {'x': x, 'cond_1152': cond_1152, 'L0_cond_W_qkv': _L0_cond_in['W_qkv'], 'L0_cond_b_qkv': _L0_cond_in['b_qkv'], 'L0_cond_W_proj': _L0_cond_in['W_proj'], 'L0_cond_b_proj': _L0_cond_in['b_proj'], 'L0_cond_W_fc1': _L0_cond_in['W_fc1'], 'L0_cond_b_fc1': _L0_cond_in['b_fc1'], 'L0_cond_W_fc2': _L0_cond_in['W_fc2'], 'L0_cond_b_fc2': _L0_cond_in['b_fc2'], 'L0_cond_W_ada': _L0_cond_in['W_ada'], 'L0_cond_b_ada': _L0_cond_in['b_ada'], 'L1_cond_ln1_w': _L1_cond_in['ln1_w'], 'L1_cond_ln1_b': _L1_cond_in['ln1_b'], 'L1_cond_wq': _L1_cond_in['wq'], 'L1_cond_wk': _L1_cond_in['wk'], 'L1_cond_wv': _L1_cond_in['wv'], 'L1_cond_wo': _L1_cond_in['wo'], 'L1_cond_wo_b': _L1_cond_in['wo_b'], 'L1_cond_ln2_w': _L1_cond_in['ln2_w'], 'L1_cond_ln2_b': _L1_cond_in['ln2_b'], 'L1_cond_fc1_w': _L1_cond_in['fc1_w'], 'L1_cond_fc1_b': _L1_cond_in['fc1_b'], 'L1_cond_fc2_w': _L1_cond_in['fc2_w'], 'L1_cond_fc2_b': _L1_cond_in['fc2_b'], 'L1_cond_ada_w': _L1_cond_in['ada_w'], 'L1_cond_ada_b': _L1_cond_in['ada_b'], 'L2_cond_qkv_w': _L2_cond_in['qkv_w'], 'L2_cond_qkv_b': _L2_cond_in['qkv_b'], 'L2_cond_proj_w': _L2_cond_in['proj_w'], 'L2_cond_proj_b': _L2_cond_in['proj_b'], 'L2_cond_fc1_w': _L2_cond_in['fc1_w'], 'L2_cond_fc1_b': _L2_cond_in['fc1_b'], 'L2_cond_fc2_w': _L2_cond_in['fc2_w'], 'L2_cond_fc2_b': _L2_cond_in['fc2_b'], 'L2_cond_ada_w': _L2_cond_in['ada_w'], 'L2_cond_ada_b': _L2_cond_in['ada_b'], 'L3_cond_qkv_w': _L3_cond_in['qkv_w'], 'L3_cond_qkv_b': _L3_cond_in['qkv_b'], 'L3_cond_out_w': _L3_cond_in['out_w'], 'L3_cond_out_b': _L3_cond_in['out_b'], 'L3_cond_w1': _L3_cond_in['w1'], 'L3_cond_b1': _L3_cond_in['b1'], 'L3_cond_w2': _L3_cond_in['w2'], 'L3_cond_b2': _L3_cond_in['b2'], 'L3_cond_ada_w': _L3_cond_in['ada_w'], 'L3_cond_ada_b': _L3_cond_in['ada_b']}

def reference(x, cond_1152, L0_cond_W_qkv, L0_cond_b_qkv, L0_cond_W_proj, L0_cond_b_proj, L0_cond_W_fc1, L0_cond_b_fc1, L0_cond_W_fc2, L0_cond_b_fc2, L0_cond_W_ada, L0_cond_b_ada, L1_cond_ln1_w, L1_cond_ln1_b, L1_cond_wq, L1_cond_wk, L1_cond_wv, L1_cond_wo, L1_cond_wo_b, L1_cond_ln2_w, L1_cond_ln2_b, L1_cond_fc1_w, L1_cond_fc1_b, L1_cond_fc2_w, L1_cond_fc2_b, L1_cond_ada_w, L1_cond_ada_b, L2_cond_qkv_w, L2_cond_qkv_b, L2_cond_proj_w, L2_cond_proj_b, L2_cond_fc1_w, L2_cond_fc1_b, L2_cond_fc2_w, L2_cond_fc2_b, L2_cond_ada_w, L2_cond_ada_b, L3_cond_qkv_w, L3_cond_qkv_b, L3_cond_out_w, L3_cond_out_b, L3_cond_w1, L3_cond_b1, L3_cond_w2, L3_cond_b2, L3_cond_ada_w, L3_cond_ada_b):
    import jax
    import jax.numpy as jnp

    def _L0_cond_ref(x, c, W_qkv, b_qkv, W_proj, b_proj, W_fc1, b_fc1, W_fc2, b_fc2, W_ada, b_ada):
        import jax, jax.numpy as jnp
        import numpy as np
        B, L, C = (8, 256, 288)
        H = 16
        D = C // H
        FF = int(C * 4.0)
        EPS = 1e-06

        def _layernorm(x):
            mu = jnp.mean(x, axis=-1, keepdims=True)
            var = jnp.mean(jnp.square(x - mu), axis=-1, keepdims=True)
            return (x - mu) * jax.lax.rsqrt(var + EPS)

        def _modulate(x, shift, scale):
            return x * (1.0 + scale) + shift

        def _attention(h, W_qkv, b_qkv, W_proj, b_proj):
            b, l, c = h.shape
            qkv = h @ W_qkv + b_qkv
            qkv = qkv.reshape(b, l, 3, H, D)
            q, k, v = (qkv[:, :, 0], qkv[:, :, 1], qkv[:, :, 2])
            scale = D ** (-0.5)
            scores = jnp.einsum('blhd,bmhd->bhlm', q * scale, k)
            attn = jax.nn.softmax(scores, axis=-1)
            o = jnp.einsum('bhlm,bmhd->blhd', attn, v).reshape(b, l, c)
            return o @ W_proj + b_proj
        ada = jax.nn.silu(c) @ W_ada + b_ada
        shift_msa, scale_msa, gate_msa, shift_mlp, scale_mlp, gate_mlp = jnp.split(ada, 6, axis=-1)
        h = _modulate(_layernorm(x), shift_msa, scale_msa)
        x = x + gate_msa * _attention(h, W_qkv, b_qkv, W_proj, b_proj)
        h = _modulate(_layernorm(x), shift_mlp, scale_mlp)
        mlp = jax.nn.gelu(h @ W_fc1 + b_fc1, approximate=True) @ W_fc2 + b_fc2
        x = x + gate_mlp * mlp
        return x

    def _L1_cond_ref(x, c, ln1_w, ln1_b, wq, wk, wv, wo, wo_b, ln2_w, ln2_b, fc1_w, fc1_b, fc2_w, fc2_b, ada_w, ada_b):
        import jax, jax.numpy as jnp
        import numpy as np
        B, S, D = (8, 256, 288)
        H = 16
        HD = D // H
        HID = int(D * 4.0)
        LN_EPS = 1e-05

        def layer_norm(x, w, b):
            m = jnp.mean(x, axis=-1, keepdims=True)
            v = jnp.mean(jnp.square(x - m), axis=-1, keepdims=True)
            return (x - m) * jax.lax.rsqrt(v + LN_EPS) * w + b

        def modulate(x, shift, scale):
            return x * (1.0 + scale[:, None, :]) + shift[:, None, :]

        def attention(x, wq, wk, wv, wo, wo_b):
            b, s, d = x.shape
            q = (x @ wq).reshape(b, s, H, HD).transpose(0, 2, 1, 3)
            k = (x @ wk).reshape(b, s, H, HD).transpose(0, 2, 1, 3)
            v = (x @ wv).reshape(b, s, H, HD).transpose(0, 2, 1, 3)
            scale = 1.0 / np.sqrt(HD).astype(np.float32)
            att = jnp.einsum('bhqd,bhkd->bhqk', q, k) * scale
            att = jax.nn.softmax(att, axis=-1)
            out = jnp.einsum('bhqk,bhkd->bhqd', att, v)
            out = out.transpose(0, 2, 1, 3).reshape(b, s, d)
            return out @ wo + wo_b
        mod = jax.nn.silu(c) @ ada_w + ada_b
        sh_msa, sc_msa, g_msa, sh_mlp, sc_mlp, g_mlp = jnp.split(mod, 6, axis=1)
        h = modulate(layer_norm(x, ln1_w, ln1_b), sh_msa, sc_msa)
        x = x + g_msa[:, None, :] * attention(h, wq, wk, wv, wo, wo_b)
        h = modulate(layer_norm(x, ln2_w, ln2_b), sh_mlp, sc_mlp)
        h = jax.nn.gelu(h @ fc1_w + fc1_b, approximate=False) @ fc2_w + fc2_b
        x = x + g_mlp[:, None, :] * h
        return x

    def _L2_cond_ref(x, c, qkv_w, qkv_b, proj_w, proj_b, fc1_w, fc1_b, fc2_w, fc2_b, ada_w, ada_b):
        import jax, jax.numpy as jnp
        import numpy as np
        N, T, D, H = (32, 256, 288, 16)
        DH = D // H
        MLP = int(D * 4.0)
        EPS = 1e-06

        def _layernorm(x):
            m = jnp.mean(x, axis=-1, keepdims=True)
            v = jnp.var(x, axis=-1, keepdims=True)
            return (x - m) * jax.lax.rsqrt(v + EPS)

        def _modulate(x, shift, scale):
            return x * (1.0 + scale[:, None, :]) + shift[:, None, :]

        def _attention(x, qkv_w, qkv_b, proj_w, proj_b):
            n, t, d = x.shape
            scale = DH ** (-0.5)
            qkv = x @ qkv_w + qkv_b
            qkv = qkv.reshape(n, t, 3, H, DH)
            q, k, v = (qkv[:, :, 0], qkv[:, :, 1], qkv[:, :, 2])
            attn = jnp.einsum('nthd,ntkd->nthk', q * scale, k)
            attn = jax.nn.softmax(attn, axis=-1)
            out = jnp.einsum('nthk,ntkd->nthd', attn, v)
            out = out.transpose(0, 2, 1, 3).reshape(n, t, d)
            return out @ proj_w + proj_b

        def _mlp(x, fc1_w, fc1_b, fc2_w, fc2_b):
            h = jax.nn.gelu(x @ fc1_w + fc1_b, approximate=False)
            return h @ fc2_w + fc2_b
        ada = jax.nn.silu(c) @ ada_w + ada_b
        shift_msa, scale_msa, gate_msa, shift_mlp, scale_mlp, gate_mlp = jnp.split(ada, 6, axis=1)
        x = x + gate_msa[:, None, :] * _attention(_modulate(_layernorm(x), shift_msa, scale_msa), qkv_w, qkv_b, proj_w, proj_b)
        x = x + gate_mlp[:, None, :] * _mlp(_modulate(_layernorm(x), shift_mlp, scale_mlp), fc1_w, fc1_b, fc2_w, fc2_b)
        return x

    def _L3_cond_ref(x, c, qkv_w, qkv_b, out_w, out_b, w1, b1, w2, b2, ada_w, ada_b):
        import math
        import jax, jax.numpy as jnp
        import numpy as np
        B, T, D = (8, 256, 288)
        H = 16
        E = 4
        EPS = 1e-06

        def _layer_norm(x):
            mu = jnp.mean(x, axis=-1, keepdims=True)
            var = jnp.mean(jnp.square(x - mu), axis=-1, keepdims=True)
            return (x - mu) * jax.lax.rsqrt(var + EPS)

        def _modulate(x, shift, scale):
            return x * (1.0 + scale) + shift

        def _attention(y, qkv_w, qkv_b, out_w, out_b):
            b, t, d = y.shape
            hd = d // H
            qkv = y @ qkv_w + qkv_b
            q, k, v = jnp.split(qkv, 3, axis=-1)
            q = q.reshape(b, t, H, hd).transpose(0, 2, 1, 3)
            k = k.reshape(b, t, H, hd).transpose(0, 2, 1, 3)
            v = v.reshape(b, t, H, hd).transpose(0, 2, 1, 3)
            scores = jnp.einsum('bhqd,bhkd->bhqk', q, k) / math.sqrt(hd)
            attn = jax.nn.softmax(scores, axis=-1)
            out = jnp.einsum('bhqk,bhkd->bhqd', attn, v)
            out = out.transpose(0, 2, 1, 3).reshape(b, t, d)
            return out @ out_w + out_b
        mods = (jax.nn.silu(c) @ ada_w + ada_b)[:, None, :]
        m0, m1, m2, m3, m4, m5 = jnp.split(mods, 6, axis=-1)
        y = _modulate(_layer_norm(x), m0, m1)
        x = x + m2 * _attention(y, qkv_w, qkv_b, out_w, out_b)
        y = _modulate(_layer_norm(x), m3, m4)
        y = jax.nn.gelu(y @ w1 + b1, approximate=True)
        x = x + m5 * (y @ w2 + b2)
        return x
    x = _L0_cond_ref(x, cond_1152[:, None, :], L0_cond_W_qkv, L0_cond_b_qkv, L0_cond_W_proj, L0_cond_b_proj, L0_cond_W_fc1, L0_cond_b_fc1, L0_cond_W_fc2, L0_cond_b_fc2, L0_cond_W_ada, L0_cond_b_ada)
    x = _L1_cond_ref(x, cond_1152, L1_cond_ln1_w, L1_cond_ln1_b, L1_cond_wq, L1_cond_wk, L1_cond_wv, L1_cond_wo, L1_cond_wo_b, L1_cond_ln2_w, L1_cond_ln2_b, L1_cond_fc1_w, L1_cond_fc1_b, L1_cond_fc2_w, L1_cond_fc2_b, L1_cond_ada_w, L1_cond_ada_b)
    x = _L2_cond_ref(x, cond_1152, L2_cond_qkv_w, L2_cond_qkv_b, L2_cond_proj_w, L2_cond_proj_b, L2_cond_fc1_w, L2_cond_fc1_b, L2_cond_fc2_w, L2_cond_fc2_b, L2_cond_ada_w, L2_cond_ada_b)
    x = _L3_cond_ref(x, cond_1152, L3_cond_qkv_w, L3_cond_qkv_b, L3_cond_out_w, L3_cond_out_b, L3_cond_w1, L3_cond_b1, L3_cond_w2, L3_cond_b2, L3_cond_ada_w, L3_cond_ada_b)
    return x

_drawn_inputs = setup_inputs


def setup_inputs(seed=0):
    import zlib

    import numpy as np

    out = dict(_drawn_inputs(seed))
    spreads = {'L0_cond_b_qkv': (0.0, 0.8),
     'L0_cond_b_proj': (0.0, 0.345),
     'L0_cond_b_fc1': (0.0, 0.8),
     'L0_cond_b_fc2': (0.0, 0.364),
     'L0_cond_b_ada': (0.0, 0.393),
     'L1_cond_ln1_w': (1.0, 0.6),
     'L1_cond_ln1_b': (0.0, 0.8),
     'L1_cond_wo_b': (0.0, 1.446),
     'L1_cond_ln2_w': (1.0, 0.6),
     'L1_cond_ln2_b': (0.0, 2.0),
     'L1_cond_fc1_b': (0.0, 2.0),
     'L1_cond_fc2_b': (0.0, 1.636),
     'L1_cond_ada_b': (0.0, 0.409),
     'L3_cond_qkv_b': (0.0, 0.8),
     'L3_cond_out_b': (0.0, 2.0),
     'L3_cond_b1': (0.0, 2.0),
     'L3_cond_b2': (0.0, 1.808),
     'L3_cond_ada_b': (0.0, 0.379)}
    factors = {'L0_cond_W_qkv': 8.0,
     'L0_cond_W_proj': 5.416,
     'L1_cond_wq': 8.0,
     'L1_cond_wk': 8.0,
     'L1_cond_wv': 8.0,
     'L1_cond_wo': 7.924,
     'L2_cond_qkv_w': 8.0,
     'L2_cond_qkv_b': 8.0,
     'L2_cond_proj_w': 8.0,
     'L2_cond_proj_b': 64.0,
     'L2_cond_fc1_b': 64.0,
     'L2_cond_fc2_b': 64.0,
     'L2_cond_ada_b': 8.0,
     'L3_cond_qkv_w': 7.953,
     'L3_cond_out_w': 5.618,
     'L1_cond_fc1_w': 3.488,
     'L2_cond_fc1_w': 8.0,
     'L2_cond_fc2_w': 8.0,
     'L3_cond_w1': 8.0,
     'L3_cond_w2': 3.337}
    for name, (base, spread) in spreads.items():
        noise = np.random.default_rng([zlib.crc32(name.encode()), seed]).standard_normal(out[name].shape)
        drawn = base * np.exp(spread * noise) if base else spread * noise
        out[name] = jnp.asarray(drawn.astype(out[name].dtype))
    for name, factor in factors.items():
        out[name] = (out[name] * factor).astype(out[name].dtype)
    return out
```

```python
from contextlib import ExitStack

import concourse.bass as bass
from concourse import mybir

ALU = mybir.AluOpType
ACT = mybir.ActivationFunctionType
AX_X = mybir.AxisListType.X
F32 = mybir.dt.float32
F32R = mybir.dt.float32r
BF16 = mybir.dt.bfloat16

P = 128
B = 2
L = 4
T = 1024
D = 288
NH = 16
HD = D // NH
FF = 4 * D
SIX = 6 * D
TT = T // P
HALF = T // 2
HT = TT // 2
REST = D - 2 * P
DX = D + 2 * REST
XROWS = 3 * REST + 2
QK = 2 * D
NM = 5
M_ROWS = [128, 128, 128, 128, 64]
FC = FF // P
TERMS = 6 * HD
SROWS = TERMS + 2
GH = 4
NG = NH // GH
VW = HD + 1
VCOLS = 320
ATTN_SCALE = float(HD) ** -0.5
CROSS = 2

N_H = 5
N_SPLIT = 18
N_AUX = NG * 64 + NG + 2 * NG
N_ST = 2 * NG * TT * 2
N_PV = NG * 2 * TT
N_STACK = 9 * 16
N_DVE = 88
N_ATTN = 17
N_CROSS = 7 * TT
N_ACT = 4
N_POOL = 24

MAX_PER_TURN = 4


def aux_order():
    order = [("max", 0)] * 64 + [("split", 0)]
    for g in range(NG):
        left = 64 if g + 1 < NG else 0
        for turn in range(2 * TT):
            if turn == 2 and g > 0:
                order.append(("output", 2 * g - 1))
            if turn == 10:
                order.append(("output", 2 * g))
            take = min(MAX_PER_TURN, left)
            order += [("max", g + 1)] * take
            left -= take
        if g + 1 < NG:
            order.append(("split", g + 1))
    return order + [("output", 2 * NG - 1)]


AUX_ORDER = aux_order()
assert len(AUX_ORDER) == N_AUX


def build_program(nc, x_in, cond, ada_w, ada_b, ln_rows, w_qkv, w_qkv_x, w_proj, w_proj_x,
                  w_fc1, w_fc1_x, w_fc2, b_fc2, out):
    mods_dram = nc.dram_tensor("mods_scratch", [B * L + 1, SIX], F32).ap()
    parts_dram = nc.dram_tensor("parts_scratch", [2, 3, D, T], BF16).ap()
    heads_dram = nc.dram_tensor("heads_scratch", [NH, T, HD], F32).ap()

    at = [(nc.sbuf_base + 31) // 32 * 32]
    limit = nc.sbuf_top

    def place(name, shape, dt, offset=None):
        size = 1
        for n in shape[1:]:
            size *= n
        size = (size * (2 if dt == BF16 else 4) + 31) // 32 * 32
        if offset is None:
            offset = at[0]
            at[0] += size
            assert at[0] <= limit, (name, at[0], limit)
        return nc.alloc_sbuf_tensor_at(name, [P] + list(shape[1:]), dt, offset=offset)

    x = place("x", [P, TT, D], F32)
    H = place("H", [P, TT, DX], F32)
    region = at[0]
    k_stack = place("k_stack", [P, NH, T], BF16)
    z_region = at[0]
    q_stack = place("q_stack", [P, NH, T], BF16)
    p_region = at[0]
    prob = place("prob", [P, 4, 2, HALF], F32)
    hid_hi = place("hid_hi", [P, FC, HALF], F32R, z_region)
    hid_lo = place("hid_lo", [P, FC, HALF], F32R, z_region + FC * HALF * 4)
    hid = place("hid", [P, 2, HALF], F32, z_region + 2 * FC * HALF * 4)
    parts = place("parts", [P, 2, 3, T], BF16, p_region)
    rest = place("rest", [P, T], F32, p_region + 12 * T)
    qkv_rows = place("qkv_rows", [P, 2, 3 * D], F32, z_region)
    products = place("products", [P, 2, NH * NH * HD], F32, z_region + 24 * D)
    head_scores = place("head_scores", [P, 2, NH, NH], F32, z_region + 24 * D + 8 * NH * NH * HD)
    head_exp = place("head_exp", [P, 2, NH, NH], F32, z_region + 24 * D + 8 * NH * NH * (HD + 1))
    head_max = place("head_max", [P, NH], F32)
    head_den = place("head_den", [P, NH], F32)
    ada_tile = place("ada_tile", [P, 2, 3, SIX], F32, region)
    mod_rows = place("mod_rows", [P, L, 6, D], F32, region + 24 * SIX)
    bias_row = place("bias_row", [P, 6, D], F32, region + 40 * SIX)
    ln_row = place("ln_row", [P, 4, D], F32, region + 44 * SIX)
    hT_hi = place("hT_hi", [P, 2, T], F32R)
    hT_lo = place("hT_lo", [P, 2, T], F32R)
    hT_x = place("hT_x", [P, T], F32R)
    wide = at[0]
    wq_hi = place("wq_hi", [P, 2, 3 * D], F32R, wide)
    wq_lo = place("wq_lo", [P, 2, 3 * D], F32R, wide + 24 * D)
    wq_x = place("wq_x", [P, 3 * D], F32R, wide + 48 * D)
    w1_hi = place("w1_hi", [P, 2, FF], F32R)
    w1_lo = place("w1_lo", [P, 2, FF], F32R)
    w1_x = place("w1_x", [P, FF], F32R)
    wp_hi = place("wp_hi", [P, 2, D], F32R)
    wp_lo = place("wp_lo", [P, 2, D], F32R)
    wp_x = place("wp_x", [P, D], F32R)
    w2_hi = place("w2_hi", [P, FC, D], F32R)
    w2_lo = place("w2_lo", [P, FC, D], F32R)
    w2_b = place("w2_b", [P, D], F32R)
    raw = place("raw", [P, 2, FF], F32)
    V = place("V", [P, TT, VCOLS], F32)
    o_T = place("o_T", [P, 2, HALF], F32)
    mods = place("mods", [P, 6, D], F32)
    ident = place("ident", [P, P], F32)
    tmp = place("tmp", [P, 2, D], F32)
    ones2 = place("ones2", [P, P], F32R)
    maxima = place("maxima", [P, 2, 64], F32)
    neg_max = place("neg_max", [P, 2, 32], F32)
    neg_parts = place("neg_parts", [P, 2, 2, P], BF16)
    stats = place("stats", [P, TT, 6], F32)
    mv = place("mv", [P, TT, 2], F32)
    var_eps = place("var_eps", [P, TT], F32)
    log_var = place("log_var", [P, TT], F32)
    rstd0 = place("rstd0", [P, TT], F32)
    newton = place("newton", [P, TT], F32)
    rstd = place("rstd", [P, TT], F32)
    inv_den = place("inv_den", [P, 2, 16], F32)
    eps = place("eps", [P, L], F32)
    cT = place("cT", [P, 3, B], F32)
    c_exp = place("c_exp", [P, 3, B], F32)
    c_silu = place("c_silu", [P, 3, B], F32)

    mod_v = mod_rows[0:B]

    with ExitStack() as ctx:
        def sem(name):
            return ctx.enter_context(nc.semaphore(name))

        ps = ctx.enter_context(nc.psum_tensor("ps", [P, 8, HALF], F32))

        c_loaded = sem("c_loaded")
        c_chain = sem("c_chain")
        ada_loaded = [sem("ada_loaded0"), sem("ada_loaded1")]
        ada_ready = sem("ada_ready")
        ada_done = sem("ada_done")
        mods_stored = sem("mods_stored")
        consts_ready = sem("consts_ready")
        raw0_loaded = sem("raw0_loaded")
        pool0 = sem("pool0")
        x_loaded = sem("x_loaded")
        x_stored = sem("x_stored")
        mods_loaded = sem("mods_loaded")
        var_ready = sem("var_ready")
        rstd_ready = sem("rstd_ready")
        h_ready = sem("h_ready")
        transposed_ready = sem("transposed_ready")
        high_done = sem("high_done")
        low_done = sem("low_done")
        qk_ready = sem("qk_ready")
        part1_done = sem("part1_done")
        rest_done = sem("rest_done")
        parts_done = sem("parts_done")
        stored = [sem("stored_even"), sem("stored_odd")]
        stack_loaded = [sem(f"stack_loaded{g}") for g in range(NG)]
        v_ready = sem("v_ready")
        v_done = sem("v_done")
        aux_ready = sem("aux_ready")
        aux_free = sem("aux_free")
        neg_max_ready = sem("neg_max_ready")
        neg_rows_loaded = sem("neg_rows_loaded")
        scores_ready = sem("scores_ready")
        exp_done = sem("exp_done")
        pv_done = sem("pv_done")
        o_copied = sem("o_copied")
        rows_copied = sem("rows_copied")
        head_scores_ready = sem("head_scores_ready")
        head_exp_done = sem("head_exp_done")
        heads_done = sem("heads_done")
        heads_stored = sem("heads_stored")
        heads_loaded = sem("heads_loaded")
        proj_ready = sem("proj_ready")
        x1_done = sem("x1_done")
        fc1_ready = sem("fc1_ready")
        gelu_done = sem("gelu_done")
        hid_hi_done = sem("hid_hi_done")
        hid_lo_done = sem("hid_lo_done")
        fc2_ready = sem("fc2_ready")
        x2_done = sem("x2_done")
        raw_loaded = [sem("raw_loaded0"), sem("raw_loaded1")]
        wq_ready = sem("wq_ready")
        wp_ready = sem("wp_ready")
        w1_ready = sem("w1_ready")
        w2_ready = sem("w2_ready")
        dve_chain = sem("dve_chain")
        dve_attn_chain = sem("dve_attn_chain")
        dve_cross_chain = sem("dve_cross_chain")
        act_chain = sem("act_chain")
        pool_chain = sem("pool_chain")

        block = ctx.enter_context(nc.Block())

        def wait_apart(eng, semaphore, value, spare):
            eng.reg_alu(spare, value - 1, 1, ALU.add)
            eng.wait_ge(pool0, 1)
            eng.wait_ge(semaphore, spare)

        def attentions_before(b, l):
            before = [l > j for j in range(L - 1) if j != CROSS]
            return b * (L - 1) + sum(before[1:], before[0])

        def counter(base):
            n = [0]

            def step():
                n[0] += 1
                return base + n[0]
            return step, n

        @block.sync
        def _(sp):
            spare = sp.alloc_register("sp_spare")
            sp.reg_mov(spare, 0)
            sp.dma_start(cT[0:96], cond).then_inc(c_loaded, 16)
            for l in range(L):
                if l >= 2:
                    sp.wait_ge(ada_ready, l - 1)
                if l >= 1:
                    sp.wait_ge(ada_done, l)
                sp.dma_start(ada_tile[0:96, l % 2], ada_w[l].rearrange("(k p) n -> p k n", p=96)).then_inc(ada_loaded[l % 2], 16)
                sp.dma_start(bias_row[0:B], ada_b[l].rearrange("(a s d) -> a s d", a=1, s=6).broadcast_to([B, 6, D])).then_inc(ada_loaded[l % 2], 16)
                sp.dma_start(ln_row[0:B], ln_rows[l:l + 1].broadcast_to([B, 4, D])).then_inc(ada_loaded[l % 2], 16)
            sp.wait_ge(ada_done, L)
            sp.dma_start(mods_dram[0:B * L].rearrange("(b l) n -> b (l n)", b=B),
                         mod_v.rearrange("b l s d -> b (l s d)")).then_inc(mods_stored, 16)
            sp.dma_start(mods_dram[B * L:B * L + 1], mod_rows[0:1, 0].rearrange("b s d -> b (s d)")).then_inc(mods_stored, 16)
            sp.wait_ge(mods_stored, 32)

            def load_mods(row):
                sp.dma_start(mods[:].rearrange("p s d -> p (s d)"),
                             mods_dram[bass.ts(row, 1), :].broadcast_to([P, SIX])).then_inc(mods_loaded, 16)

            load_mods(0)

            with sp.Fori(0, B) as b:
                sp.dma_start(x[:], x_in[bass.ts(b, 1)].rearrange("b (t p) d -> p (b t) d", p=P)).then_inc(x_loaded, 16)
                with sp.Fori(0, L) as l:
                    it = b * L + l
                    at = attentions_before(b, l)
                    with sp.If(l != CROSS):
                        for m in range(NM):
                            sp.wait_ge(parts_done, at * NM + m + 1)
                            r0 = m * P
                            for which in range(2):
                                lo, hi = max(r0, which * D), min(r0 + M_ROWS[m], (which + 1) * D)
                                if lo < hi:
                                    sp.dma_start(parts_dram[which, :, lo - which * D:hi - which * D, :].rearrange("j r t -> r j t"),
                                                 parts[lo - r0:hi - r0, m % 2]).then_inc(stored[m % 2], 16)
                        sp.wait_ge(stored[0], at * 64 + 64)
                        sp.wait_ge(stored[1], at * 32 + 32)
                        for g in range(NG):
                            heads = slice(g * GH, (g + 1) * GH)
                            rows = parts_dram.rearrange("w j (r h) t -> w (j r) h t", h=NH)
                            for n, (r0, parts_of_k) in enumerate(((0, 3), (3, 2), (5, 1))):
                                sp.dma_start(k_stack[r0 * HD:(r0 + parts_of_k) * HD, heads, :],
                                             rows[1, 0:parts_of_k * HD, heads, :]).then_inc(stack_loaded[g], 16)
                                for i in range(r0, r0 + parts_of_k):
                                    sp.dma_start(q_stack[i * HD:(i + 1) * HD, heads, :],
                                                 rows[0, n * HD:(n + 1) * HD, heads, :]).then_inc(stack_loaded[g], 16)
                        for g in range(NG):
                            sp.wait_ge(aux_free, at * N_AUX + AUX_ORDER.index(("split", g)) + 1)
                            for j in range(2):
                                row = q_stack[TERMS + j:TERMS + j + 1, g * GH:(g + 1) * GH, :]
                                sp.dma_start(row.rearrange("p h (a t) -> p (h a) t", t=P),
                                             neg_parts[0:32, g % 2, j]).then_inc(neg_rows_loaded, 16)
                    with sp.Else():
                        for t in range(TT):
                            sp.wait_ge(heads_done, b * TT + t + 1)
                            sp.dma_start(heads_dram[:, t * P:(t + 1) * P, :].rearrange("h p c -> p h c"),
                                         H[:, t, 0:D].rearrange("p (h c) -> p h c", h=NH)).then_inc(heads_stored, 16)
                        sp.wait_ge(heads_stored, b * 16 * TT + 16 * TT)
                        sp.dma_start(H[:, :, 0:D], heads_dram.rearrange("h (r s) c -> (h r) (s c)", s=NH)
                                     .rearrange("(t p) n -> p t n", p=P)).then_inc(heads_loaded, 16)
                    sp.wait_ge(x2_done, it * TT + TT)
                    load_mods(it + 1)
                sp.dma_start(out[bass.ts(b, 1)].rearrange("b (t p) d -> p (b t) d", p=P), x[:]).then_inc(x_stored, 16)
                wait_apart(sp, x_stored, b * 16 + 16, spare)
            sp.wait_ge(mods_loaded, (B * L + 1) * 16)

        @block.gpsimd
        def _(pool):
            spare = pool.alloc_register("pool_spare")
            pool.reg_mov(spare, 0)
            step0, _ = counter(0)

            nc.gpsimd.memset(ident[:], 0.0).then_inc(pool0, 1)
            pool.wait_ge(pool0, step0())
            nc.gpsimd.affine_select(out=ident[:], in_=ident[:], compare_op=ALU.not_equal, fill=1.0,
                                    base=0, pattern=[[-1, P]], channel_multiplier=1).then_inc(pool0, 1)
            pool.wait_ge(pool0, step0())
            nc.gpsimd.memset(ones2[0:2].bitcast(F32), 1.0).then_inc(pool0, 1)
            pool.wait_ge(pool0, step0())
            nc.gpsimd.memset(hT_x[3 * REST:XROWS].bitcast(F32), 1.0).then_inc(pool0, 1)
            pool.wait_ge(pool0, step0())
            nc.gpsimd.memset(V[:], 1.0).then_inc(pool0, 1)
            pool.wait_ge(pool0, step0())
            nc.gpsimd.memset(eps[:], 1e-6).then_inc(pool0, 1)
            pool.wait_ge(pool0, step0())
            nc.gpsimd.memset(eps[:, 1:2], 1e-5).then_inc(pool0, 1)
            pool.wait_ge(pool0, step0())

            def split_main(own, step, hi, lo, src):
                nc.gpsimd.tensor_copy(hi, src).then_inc(own, 1)
                pool.wait_ge(own, step())
                nc.gpsimd.tensor_tensor(lo, src, hi.bitcast(F32), ALU.subtract).then_inc(own, 1)
                pool.wait_ge(own, step())

            def split_x(own, step, dst, src, ready, count):
                nc.gpsimd.tensor_copy(dst[0:XROWS], src[0:XROWS]).then_inc(own, 1)
                pool.wait_ge(own, step())
                nc.gpsimd.tensor_tensor(dst[64:XROWS], src[64:XROWS], dst[64:XROWS].bitcast(F32),
                                        ALU.subtract).then_inc(own, 1)
                wait_apart(pool, own, step(), spare)
                nc.gpsimd.tensor_copy(dst[96:97], src[96:97]).then_inc(ready, 1)
                pool.wait_ge(ready, count)

            for i in range(3):
                piece = raw[:, i % 2, 0:3 * D]
                if i < 2:
                    pool.dma_start(piece, w_qkv[0, i]).then_inc(raw0_loaded, 16)
                else:
                    pool.dma_start(piece[0:XROWS], w_qkv_x[0]).then_inc(raw0_loaded, 16)
                pool.wait_ge(raw0_loaded, 16 * (i + 1))
                if i < 2:
                    split_main(pool0, step0, wq_hi[:, i], wq_lo[:, i], piece)
                else:
                    split_x(pool0, step0, wq_x, piece, wq_ready, 1)
            pool.wait_ge(mods_stored, 32)
            nc.gpsimd.memset(k_stack[3 * REST:SROWS], 1.0).then_inc(consts_ready, 1)

            with pool.Fori(0, B) as b:
                with pool.Fori(0, L) as l:
                    it = b * L + l
                    at = attentions_before(b, l)
                    step, steps = counter(it * N_POOL)

                    def load(i):
                        this, following = bass.ts(l, 1), bass.ts(l + 1, 1)
                        half = raw[:, i % 2]
                        if i == 0:
                            dst, src = half[:, 0:2 * D].rearrange("p (c n) -> p c n", c=2), w_proj[this].rearrange("l c p n -> p (l c) n")
                        elif i == 1:
                            dst, src = half[0:XROWS, 0:D], w_proj_x[this].rearrange("l p n -> p (l n)")
                        elif i < 4:
                            dst, src = half, w_fc1[this, i - 2].rearrange("l p n -> p (l n)")
                        elif i == 4:
                            dst, src = half[0:XROWS], w_fc1_x[this].rearrange("l p n -> p (l n)")
                        elif i < 8:
                            dst = half[:, 0:3 * D].rearrange("p (c n) -> p c n", c=3)
                            src = w_fc2[this, 3 * (i - 5):3 * (i - 4)].rearrange("l c p n -> p (l c) n")
                        elif i == 8:
                            dst, src = half[0:2, 0:D], b_fc2[this].rearrange("l p n -> p (l n)")
                        elif i < 11:
                            dst, src = half[:, 0:3 * D], w_qkv[following, i - 9].rearrange("l p n -> p (l n)")
                        else:
                            dst, src = half[0:XROWS, 0:3 * D], w_qkv_x[following].rearrange("l p n -> p (l n)")
                        pool.dma_start(dst, src).then_inc(raw_loaded[i % 2], 16)

                    load(0)
                    load(1)
                    pool.wait_ge(v_ready, it * TT + TT)
                    for i in range(12):
                        piece = raw[:, i % 2]
                        wait_apart(pool, raw_loaded[i % 2], it * 96 + 16 * (i // 2 + 1), spare)
                        if i == 0:
                            split_main(pool_chain, step, wp_hi[:].rearrange("p c n -> p (c n)"),
                                       wp_lo[:].rearrange("p c n -> p (c n)"), piece[:, 0:2 * D])
                        elif i == 1:
                            split_x(pool_chain, step, wp_x, piece[:, 0:D], wp_ready, it + 1)
                        elif i < 4:
                            split_main(pool_chain, step, w1_hi[:, i - 2], w1_lo[:, i - 2], piece)
                        elif i == 4:
                            split_x(pool_chain, step, w1_x, piece, w1_ready, it + 1)
                        elif i < 8:
                            cs = slice(3 * (i - 5), 3 * (i - 4))
                            split_main(pool_chain, step, w2_hi[:, cs].rearrange("p c n -> p (c n)"),
                                       w2_lo[:, cs].rearrange("p c n -> p (c n)"), piece[:, 0:3 * D])
                        elif i == 8:
                            nc.gpsimd.tensor_copy(w2_b[0:2], piece[0:2, 0:D]).then_inc(pool_chain, 1)
                            pool.wait_ge(pool_chain, step())
                            nc.gpsimd.tensor_tensor(w2_b[0:2], piece[0:2, 0:D], w2_b[0:2].bitcast(F32), ALU.subtract).then_inc(pool_chain, 1)
                            wait_apart(pool, pool_chain, step(), spare)
                            nc.gpsimd.tensor_copy(w2_b[0:1], piece[0:1, 0:D]).then_inc(w2_ready, 1)
                            pool.wait_ge(w2_ready, it + 1)
                        elif i < 11:
                            split_main(pool_chain, step, wq_hi[:, i - 9], wq_lo[:, i - 9], piece[:, 0:3 * D])
                        else:
                            split_x(pool_chain, step, wq_x, piece[:, 0:3 * D], wq_ready, it + 2)
                        if i + 2 < 12:
                            load(i + 2)
                        if i == 8:
                            pool.wait_ge(fc1_ready, it * 2 * FC + 2 * FC)
                    assert steps == [N_POOL], steps

        @block.scalar
        def _(act):
            act.wait_ge(c_loaded, 16)
            nc.scalar.activation(c_exp[0:96], cT[0:96], ACT.Exp, scale=-1.0).then_inc(c_chain, 1)

            with act.Fori(0, B) as b:
                with act.Fori(0, L) as l:
                    it = b * L + l
                    at = attentions_before(b, l)
                    step, steps = counter(it * N_ACT)

                    def first_rstd(use, half):
                        ts = slice(half * HT, (half + 1) * HT)
                        act.wait_ge(var_ready, it * 4 + 2 * use + half + 1)
                        nc.scalar.activation(log_var[:, ts], var_eps[:, ts], ACT.Ln).then_inc(act_chain, 1)
                        act.wait_ge(act_chain, step())
                        nc.scalar.activation(rstd0[:, ts], log_var[:, ts], ACT.Exp, scale=-0.5).then_inc(rstd_ready, 1)

                    def high_parts(use):
                        for half in range(2):
                            cols = slice(half * HALF, (half + 1) * HALF)
                            for c in range(3):
                                act.wait_ge(transposed_ready, it * N_SPLIT + 6 * use + 3 * half + c + 1)
                                bank = 3 * half + c
                                if c < 2:
                                    ins = nc.scalar.copy(hT_hi[:, c, cols], ps[:, bank])
                                else:
                                    ins = nc.scalar.copy(hT_x[0:3 * REST, cols], ps[0:3 * REST, bank])
                                ins.then_inc(high_done, 1)

                    def exp_heads(t):
                        act.wait_ge(head_scores_ready, b * TT + t + 1)
                        if t >= 2:
                            act.wait_ge(heads_done, b * TT + t - 1)
                        nc.scalar.activation(head_exp[:, t % 2], head_scores[:, t % 2], ACT.Exp,
                                             scale=ATTN_SCALE).then_inc(head_exp_done, 1)

                    first_rstd(0, 0)
                    first_rstd(0, 1)
                    high_parts(0)
                    with act.If(l != CROSS):
                        for m in range(NM):
                            rows = M_ROWS[m]
                            pair = (3, 0, 1, 2, 3)[m]
                            act.wait_ge(qk_ready, at * NM + m + 1)
                            if m >= 2:
                                act.wait_ge(stored[m % 2], at * (64, 32)[m % 2] + (16, 16, 48)[(m - 2)] if m != 3 else at * 32 + 16)
                            nc.scalar.copy(parts[0:rows, m % 2, 0].rearrange("p (n t) -> p n t", n=2),
                                           ps[0:rows, 2 * pair:2 * pair + 2]).then_inc(part1_done, 1)
                        for t in range(TT):
                            act.wait_ge(v_ready, it * TT + t + 1)
                            nc.scalar.copy(V[:, t, 0:NH * VW].rearrange("p (h c) -> p h c", h=NH)[:, :, 0:HD],
                                           ps[:, t, 0:D].rearrange("p (h c) -> p h c", h=NH)).then_inc(v_done, 1)
                        def copy_output(i):
                            act.wait_ge(pv_done, at * N_PV + TT * (i + 1))
                            if i >= 2:
                                act.wait_ge(aux_ready, at * N_AUX + AUX_ORDER.index(("output", i - 2)) + 1)
                            nc.scalar.copy(o_T[:, i % 2], ps[:, 6 + i % 2]).then_inc(o_copied, 1)

                        for u in range(N_ST):
                            act.wait_ge(scores_ready, at * N_ST + u + 1)
                            if u >= 4:
                                act.wait_ge(pv_done, at * N_PV + u // 2 - 1)
                            nc.scalar.activation(prob[:, u % 4], ps[:, 2 * (u % 2):2 * (u % 2) + 2], ACT.Exp,
                                                 scale=ATTN_SCALE).then_inc(exp_done, 1)
                            if u % (2 * TT) == 1 and u > 2 * TT:
                                copy_output(u // (2 * TT) - 1)
                        copy_output(2 * NG - 1)
                    with act.Else():
                        for t in range(TT):
                            act.wait_ge(v_ready, it * TT + t + 1)
                            if t >= 2:
                                act.wait_ge(heads_done, b * TT + t - 1)
                            nc.scalar.copy(qkv_rows[:, t % 2].rearrange("p (n c) -> p n c", n=2),
                                           ps[:, 2 * (t % 4):2 * (t % 4) + 2, 0:3 * D // 2]).then_inc(rows_copied, 1)
                            if t >= 1:
                                exp_heads(t - 1)
                        exp_heads(TT - 1)
                    high_parts(1)
                    first_rstd(1, 0)
                    first_rstd(1, 1)
                    high_parts(2)
                    def gelu(i, func):
                        act.wait_ge(fc1_ready, it * 2 * FC + i + 1)
                        if i >= 2:
                            act.wait_ge(hid_lo_done, it * 2 * FC + i - 1)
                        nc.scalar.activation(hid[:, i % 2], ps[:, 6 + i % 2], func).then_inc(gelu_done, 1)
                        act.wait_ge(gelu_done, it * 2 * FC + i + 1)
                        if i == FC:
                            act.wait_ge(fc2_ready, it * TT + HT)
                        nc.scalar.copy(hid_hi[:, i % FC], hid[:, i % 2]).then_inc(hid_hi_done, 1)

                    with act.If(l * (L - 1 - l) < 1):
                        for i in range(2 * FC):
                            gelu(i, ACT.Gelu_apprx_tanh)
                    with act.Else():
                        for i in range(2 * FC):
                            gelu(i, ACT.Gelu)
                    assert steps == [N_ACT], steps

        @block.vector
        def _(dve):
            spare = dve.alloc_register("dve_spare")
            dve.reg_mov(spare, 0)
            dve.wait_ge(c_chain, 1)
            nc.vector.tensor_scalar(c_exp[0:96], c_exp[0:96], 1.0, None, ALU.add).then_inc(c_chain, 1)
            dve.wait_ge(c_chain, 2)
            nc.vector.reciprocal(c_exp[0:96], c_exp[0:96]).then_inc(c_chain, 1)
            dve.wait_ge(c_chain, 3)
            nc.vector.tensor_tensor(c_silu[0:96], cT[0:96], c_exp[0:96], ALU.mult).then_inc(c_chain, 1)
            n = 4
            for l in range(L):
                dve.wait_ge(ada_loaded[l % 2], 48 * (l // 2 + 1))
                dve.wait_ge(ada_ready, l + 1)
                flat = mod_v[:, l].rearrange("b s d -> b (s d)")
                for j in range(4):
                    cols = slice(j * SIX // 4, (j + 1) * SIX // 4)
                    nc.vector.tensor_tensor(flat[:, cols], ps[0:B, 4 * (l % 2) + j, 0:SIX // 4],
                                            bias_row[0:B].rearrange("b s d -> b (s d)")[:, cols], ALU.add).then_inc(c_chain, 1)
                    n += 1
                dve.wait_ge(c_chain, n)
                scale, shift = mod_v[:, l, 1:5:3], mod_v[:, l, 0:4:3]
                work = tmp[0:B]
                for ins in (lambda: nc.vector.tensor_scalar(scale, scale, 1.0, None, ALU.add),
                            lambda: nc.vector.tensor_tensor(work, scale, ln_row[0:B, 2:4], ALU.mult),
                            lambda: nc.vector.tensor_tensor(shift, shift, work, ALU.add)):
                    ins().then_inc(c_chain, 1)
                    n += 1
                    dve.wait_ge(c_chain, n)
                nc.vector.tensor_tensor(scale, scale, ln_row[0:B, 0:2], ALU.mult).then_inc(ada_done, 1)
                dve.wait_ge(ada_done, l + 1)
            dve.wait_ge(pool0, 7)

            with dve.Fori(0, B) as b:
                with dve.Fori(0, L) as l:
                    it = b * L + l
                    at = attentions_before(b, l)
                    step, steps = counter(it * N_DVE)

                    def norm_stats(use, half):
                        for t in range(half * HT, (half + 1) * HT):
                            nc.vector.bn_stats(stats[:, t], x[:, t]).then_inc(dve_chain, 1)
                            last = step()
                        wait_apart(dve, dve_chain, last, spare)
                        for t in range(half * HT, (half + 1) * HT):
                            nc.vector.bn_aggr(mv[:, t], stats[:, t]).then_inc(dve_chain, 1)
                            last = step()
                        dve.wait_ge(dve_chain, last)
                        ts = slice(half * HT, (half + 1) * HT)
                        nc.vector.tensor_scalar(var_eps[:, ts], mv[:, ts, 1], eps[:, bass.ts(l, 1)], None,
                                                ALU.add).then_inc(var_ready, 1)

                    def normalize(use, half):
                        ts = slice(half * HT, (half + 1) * HT)
                        dve.wait_ge(var_ready, it * 4 + 2 * use + half + 1)
                        dve.wait_ge(rstd_ready, it * 4 + 2 * use + half + 1)
                        nc.vector.tensor_tensor(newton[:, ts], rstd0[:, ts], rstd0[:, ts], ALU.mult).then_inc(dve_chain, 1)
                        dve.wait_ge(dve_chain, step())
                        nc.vector.tensor_tensor(newton[:, ts], newton[:, ts], var_eps[:, ts], ALU.mult).then_inc(dve_chain, 1)
                        dve.wait_ge(dve_chain, step())
                        nc.vector.tensor_scalar(newton[:, ts], newton[:, ts], -0.5, 1.5, ALU.mult, ALU.add).then_inc(dve_chain, 1)
                        dve.wait_ge(dve_chain, step())
                        nc.vector.tensor_tensor(rstd[:, ts], rstd0[:, ts], newton[:, ts], ALU.mult).then_inc(dve_chain, 1)
                        dve.wait_ge(dve_chain, step())
                        for t in range(half * HT, (half + 1) * HT):
                            nc.vector.tensor_scalar(H[:, t, 0:D], x[:, t], mv[:, t, 0:1], rstd[:, t:t + 1],
                                                    ALU.subtract, ALU.mult).then_inc(dve_chain, 1)
                            last = step()
                        dve.wait_ge(dve_chain, last)
                        rows = H[:, ts, 0:D]
                        nc.vector.tensor_tensor(
                            rows, rows, mods[:, 3 * use + 1].unsqueeze(1).broadcast_to([P, HT, D]), ALU.mult).then_inc(dve_chain, 1)
                        dve.wait_ge(dve_chain, step())
                        nc.vector.tensor_tensor(
                            rows, rows, mods[:, 3 * use].unsqueeze(1).broadcast_to([P, HT, D]), ALU.add).then_inc(dve_chain, 1)
                        dve.wait_ge(dve_chain, step())
                        repeat_last(ts, HT)

                    def repeat_last(ts, count):
                        nc.vector.tensor_copy(
                            H[:, ts, D:DX].rearrange("p t (a c) -> p t a c", a=2),
                            H[:, ts, D - REST:D].unsqueeze(2).broadcast_to([P, count, 2, REST])).then_inc(h_ready, 1)

                    def low_parts(use):
                        for half in range(2):
                            cols = slice(half * HALF, (half + 1) * HALF)
                            for c in range(3):
                                dve.wait_ge(high_done, it * N_SPLIT + 6 * use + 3 * half + c + 1)
                                bank = 3 * half + c
                                if c < 2:
                                    ins = nc.vector.tensor_tensor(hT_lo[:, c, cols], ps[:, bank],
                                                                  hT_hi[:, c, cols].bitcast(F32), ALU.subtract)
                                else:
                                    mid = hT_x[REST:2 * REST, cols]
                                    ins = nc.vector.tensor_tensor(mid, ps[REST:2 * REST, bank], mid.bitcast(F32), ALU.subtract)
                                ins.then_inc(low_done, 1)

                    def add_gated(t, bank, gate, done):
                        nc.vector.tensor_tensor(tmp[:, t % 2], ps[:, bank, 0:D], mods[:, gate], ALU.mult).then_inc(dve_chain, 1)
                        dve.wait_ge(dve_chain, step())
                        nc.vector.tensor_tensor(x[:, t], x[:, t], tmp[:, t % 2], ALU.add).then_inc(done, 1)

                    dve.wait_ge(x_loaded, b * 16 + 16)
                    dve.wait_ge(mods_loaded, it * 16 + 16)
                    norm_stats(0, 0)
                    norm_stats(0, 1)
                    normalize(0, 0)
                    normalize(0, 1)
                    low_parts(0)
                    with dve.If(l != CROSS):
                        attn_step, attn_steps = counter(at * N_ATTN)
                        for m in range(NM):
                            rows = M_ROWS[m]
                            pair = (3, 0, 1, 2, 3)[m]
                            dve.wait_ge(part1_done, at * NM + m + 1)
                            part = [parts[0:rows, m % 2, j] for j in range(3)]
                            left = rest[0:rows]
                            nc.vector.tensor_tensor(left.rearrange("p (n t) -> p n t", n=2), ps[0:rows, 2 * pair:2 * pair + 2],
                                                    part[0].rearrange("p (n t) -> p n t", n=2), ALU.subtract).then_inc(rest_done, 1)
                            dve.wait_ge(rest_done, at * NM + m + 1)
                            nc.vector.tensor_copy(part[1], left).then_inc(dve_attn_chain, 1)
                            dve.wait_ge(dve_attn_chain, attn_step())
                            nc.vector.tensor_tensor(part[2], left, part[1], ALU.subtract).then_inc(parts_done, 1)
                            dve.wait_ge(parts_done, at * NM + m + 1)
                        use = [0]

                        def maximum(g, i):
                            dve.wait_ge(aux_ready, at * N_AUX + use[0] + 1)
                            nc.vector.reduce_max(maxima[:, g % 2, i:i + 1], ps[:, 4 + use[0] % 2], AX_X).then_inc(aux_free, 1)
                            use[0] += 1

                        def negate_maxima(g):
                            dve.wait_ge(aux_free, at * N_AUX + use[0])
                            nc.vector.reduce_max(neg_max[:, g % 2], maxima[:, g % 2].rearrange("p (a h) -> p a h", h=2),
                                                 AX_X, negate=True).then_inc(neg_max_ready, 1)
                            dve.wait_ge(neg_max_ready, at * NG + g + 1)

                        def split_maxima(g):
                            dve.wait_ge(aux_ready, at * N_AUX + use[0] + 1)
                            src = ps[0:32, 4 + use[0] % 2, 0:P]
                            nc.vector.tensor_copy(neg_parts[0:32, g % 2, 0], src).then_inc(dve_attn_chain, 1)
                            dve.wait_ge(dve_attn_chain, attn_step())
                            nc.vector.tensor_tensor(neg_parts[0:32, g % 2, 1], src, neg_parts[0:32, g % 2, 0],
                                                    ALU.subtract).then_inc(aux_free, 1)
                            use[0] += 1

                        def output(i):
                            g, half = i // 2, i % 2
                            dve.wait_ge(aux_ready, at * N_AUX + use[0] + 1)
                            src = ps[:, 4 + use[0] % 2].rearrange("p (t h c) -> p t h c", t=HT, h=GH)
                            inv = inv_den[:, half].rearrange("p (t h c) -> p t h c", t=HT, h=GH)
                            nc.vector.reciprocal(inv, src[:, :, :, HD:VW]).then_inc(dve_attn_chain, 1)
                            dve.wait_ge(dve_attn_chain, attn_step())
                            nc.vector.tensor_tensor(
                                H[:, half * HT:(half + 1) * HT, g * GH * HD:(g + 1) * GH * HD].rearrange("p t (h c) -> p t h c", h=GH),
                                src[:, :, :, 0:HD], inv.broadcast_to([P, HT, GH, HD]), ALU.mult).then_inc(aux_free, 1)
                            use[0] += 1

                        for i in range(64):
                            maximum(0, i)
                        negate_maxima(0)
                        split_maxima(0)
                        for g in range(NG):
                            left = 64 if g + 1 < NG else 0
                            for turn in range(2 * TT):
                                if turn == 2 and g > 0:
                                    output(2 * g - 1)
                                if turn == 10:
                                    output(2 * g)
                                for _ in range(min(MAX_PER_TURN, left)):
                                    maximum(g + 1, 64 - left)
                                    left -= 1
                            if g + 1 < NG:
                                negate_maxima(g + 1)
                                split_maxima(g + 1)
                        output(2 * NG - 1)
                        wait_apart(dve, aux_free, at * N_AUX + N_AUX, spare)
                        assert attn_steps == [N_ATTN], attn_steps
                    with dve.Else():
                        cross_step, cross_steps = counter(b * N_CROSS)

                        def head_scores_of(t):
                            q, k = (qkv_rows[:, t % 2, w * D:(w + 1) * D].rearrange("p (h c) -> p h c", h=NH) for w in range(2))
                            work = products[:, 0].rearrange("p (h k c) -> p h k c", h=NH, k=NH)
                            dve.wait_ge(rows_copied, b * TT + t + 1)
                            nc.vector.tensor_tensor(work, q.unsqueeze(2).broadcast_to([P, NH, NH, HD]),
                                                    k.unsqueeze(1).broadcast_to([P, NH, NH, HD]), ALU.mult).then_inc(dve_cross_chain, 1)
                            dve.wait_ge(dve_cross_chain, cross_step())
                            nc.vector.tensor_reduce(head_scores[:, t % 2], work, AX_X, ALU.add).then_inc(dve_cross_chain, 1)
                            dve.wait_ge(dve_cross_chain, cross_step())
                            nc.vector.reduce_max(head_max[:], head_scores[:, t % 2], AX_X).then_inc(dve_cross_chain, 1)
                            dve.wait_ge(dve_cross_chain, cross_step())
                            nc.vector.tensor_tensor(head_scores[:, t % 2], head_scores[:, t % 2],
                                                    head_max[:].unsqueeze(2).broadcast_to([P, NH, NH]),
                                                    ALU.subtract).then_inc(head_scores_ready, 1)

                        def head_outputs(t):
                            v = qkv_rows[:, t % 2, 2 * D:3 * D].rearrange("p (k c) -> p c k", k=NH)
                            work = products[:, 1].rearrange("p (h c k) -> p h c k", h=NH, c=HD)
                            o = H[:, t, 0:D].rearrange("p (h c) -> p h c", h=NH)
                            dve.wait_ge(head_exp_done, b * TT + t + 1)
                            nc.vector.tensor_tensor(work, head_exp[:, t % 2].unsqueeze(2).broadcast_to([P, NH, HD, NH]),
                                                    v.unsqueeze(1).broadcast_to([P, NH, HD, NH]), ALU.mult).then_inc(dve_cross_chain, 1)
                            dve.wait_ge(dve_cross_chain, cross_step())
                            nc.vector.tensor_reduce(o, work, AX_X, ALU.add).then_inc(dve_cross_chain, 1)
                            dve.wait_ge(dve_cross_chain, cross_step())
                            nc.vector.tensor_reduce(head_den[:], head_exp[:, t % 2], AX_X, ALU.add).then_inc(dve_cross_chain, 1)
                            dve.wait_ge(dve_cross_chain, cross_step())
                            nc.vector.reciprocal(head_den[:], head_den[:]).then_inc(dve_cross_chain, 1)
                            dve.wait_ge(dve_cross_chain, cross_step())
                            nc.vector.tensor_tensor(o, o, head_den[:].unsqueeze(2).broadcast_to([P, NH, HD]),
                                                    ALU.mult).then_inc(heads_done, 1)

                        for t in range(TT):
                            head_scores_of(t)
                            if t >= 1:
                                head_outputs(t - 1)
                        head_outputs(TT - 1)
                        wait_apart(dve, heads_loaded, b * 16 + 16, spare)
                        assert cross_steps == [N_CROSS], cross_steps
                    repeat_last(slice(0, TT), TT)
                    low_parts(1)
                    for half in range(2):
                        for t in range(half * HT, (half + 1) * HT):
                            dve.wait_ge(proj_ready, it * TT + t + 1)
                            add_gated(t, (6, 7, 0, 1, 2, 3, 4, 5)[t], 2, x1_done)
                        dve.wait_ge(x1_done, it * TT + (half + 1) * HT)
                        norm_stats(1, half)
                    normalize(1, 0)
                    normalize(1, 1)
                    low_parts(2)
                    for half in range(2):
                        for i in range(half * FC, (half + 1) * FC):
                            dve.wait_ge(hid_hi_done, it * 2 * FC + i + 1)
                            nc.vector.tensor_tensor(hid_lo[:, i % FC], hid[:, i % 2], hid_hi[:, i % FC].bitcast(F32),
                                                    ALU.subtract).then_inc(hid_lo_done, 1)
                        for t in range(half * HT, (half + 1) * HT):
                            dve.wait_ge(fc2_ready, it * TT + t + 1)
                            add_gated(t, t % 6, 5, x2_done)
                    dve.wait_ge(x2_done, it * TT + TT)
                    assert steps == [N_DVE], steps

        @block.tensor
        def _(pe):
            pe.wait_ge(c_chain, 4)
            for l in range(L):
                pe.wait_ge(ada_loaded[l % 2], 48 * (l // 2 + 1))
                if l >= 2:
                    pe.wait_ge(ada_done, l - 1)
                for j in range(4):
                    for k in range(3):
                        ins = nc.tensor.matmul(ps[0:B, 4 * (l % 2) + j, 0:SIX // 4], c_silu[0:96, k],
                                               ada_tile[0:96, l % 2, k, j * SIX // 4:(j + 1) * SIX // 4],
                                               start=(k == 0), stop=(k == 2))
                ins.then_inc(ada_ready, 1)
            pe.wait_ge(pool0, 7)
            pe.wait_ge(consts_ready, 1)
            pe.wait_ge(ada_done, L)

            with pe.Fori(0, B) as b:
                with pe.Fori(0, L) as l:
                    it = b * L + l
                    at = attentions_before(b, l)

                    def transpose_h(use, half, h_value):
                        pe.wait_ge(h_ready, it * N_H + h_value)
                        for c in range(3):
                            width = P if c < 2 else 3 * REST
                            for t in range(HT):
                                ins = nc.tensor.transpose(ps[0:width, 3 * half + c, t * P:(t + 1) * P],
                                                          H[:, half * HT + t, c * P:c * P + width], ident[:])
                            ins.then_inc(transposed_ready, 1)

                    def split_done(use, half):
                        pe.wait_ge(low_done, it * N_SPLIT + 6 * use + 3 * half + 3)

                    def product(dst, stationary, moving):
                        for n, (s, m) in enumerate(zip(stationary, moving)):
                            ins = nc.tensor.matmul(dst, s, m, start=(n == 0), stop=(n == len(stationary) - 1))
                        return ins

                    def acts(cols):
                        out_ = []
                        for c in range(2):
                            out_ += [hT_hi[:, c, cols], hT_lo[:, c, cols], hT_hi[:, c, cols]]
                        return out_ + [hT_x[0:XROWS, cols]]

                    def weights(hi, lo, x_, cols):
                        out_ = []
                        for c in range(2):
                            out_ += [hi[:, c, cols], hi[:, c, cols], lo[:, c, cols]]
                        return out_ + [x_[0:XROWS, cols]]

                    transpose_h(0, 0, 1)
                    transpose_h(0, 1, 2)
                    pe.wait_ge(wq_ready, it + 1)
                    with pe.If(l != CROSS):
                        for m in range(NM):
                            rows = M_ROWS[m]
                            pair = (3, 0, 1, 2, 3)[m]
                            if m == 4:
                                pe.wait_ge(rest_done, at * NM + 1)
                            for n in range(2):
                                if m == 0:
                                    split_done(0, n)
                                ins = product(ps[0:rows, 2 * pair + n], weights(wq_hi, wq_lo, wq_x, slice(m * P, m * P + rows)),
                                              acts(slice(n * HALF, (n + 1) * HALF)))
                            ins.then_inc(qk_ready, 1)
                        for t in range(TT):
                            if t % 2 == 0:
                                pe.wait_ge(rest_done, at * NM + 2 + t // 2)
                            product(ps[:, t, 0:D], acts(slice(t * P, (t + 1) * P)),
                                    weights(wq_hi, wq_lo, wq_x, slice(QK, QK + D))).then_inc(v_ready, 1)

                        use = [0]

                        def aux_bank():
                            n = use[0]
                            if n == 0:
                                pe.wait_ge(v_done, at * TT + 6)
                            elif n >= 2:
                                pe.wait_ge(aux_free, at * N_AUX + n - 1)
                            use[0] += 1
                            return 4 + n % 2

                        def maximum(g, i):
                            if i == 0:
                                pe.wait_ge(stack_loaded[g], at * N_STACK + N_STACK)
                            head, tile, half = g * GH + i // 16, i // 2 % 8, i % 2
                            nc.tensor.matmul(ps[:, aux_bank()], q_stack[0:TERMS, head, tile * P:(tile + 1) * P],
                                             k_stack[0:TERMS, head, half * HALF:(half + 1) * HALF],
                                             start=True, stop=True).then_inc(aux_ready, 1)

                        def transpose_maxima(g):
                            pe.wait_ge(neg_max_ready, at * NG + g + 1)
                            nc.tensor.transpose(ps[0:32, aux_bank(), 0:P], neg_max[:, g % 2], ident[:]).then_inc(aux_ready, 1)

                        def transpose_output(i):
                            pe.wait_ge(o_copied, at * 2 * NG + i + 1)
                            bank = aux_bank()
                            for t in range(HT):
                                ins = nc.tensor.transpose(ps[:, bank, t * P:(t + 1) * P], o_T[:, i % 2, t * P:(t + 1) * P], ident[:])
                            ins.then_inc(aux_ready, 1)

                        def scores(g, half, kc, pair):
                            u = ((g * 2 + half) * TT + kc) * 2 + pair
                            if u == 0:
                                pe.wait_ge(v_done, at * TT + 4)
                            elif u >= 2:
                                pe.wait_ge(exp_done, at * N_ST + u - 1)
                            for j in range(2):
                                head = g * GH + 2 * pair + j
                                ins = nc.tensor.matmul(ps[:, 2 * (u % 2) + j], k_stack[0:SROWS, head, kc * P:(kc + 1) * P],
                                                       q_stack[0:SROWS, head, half * HALF:(half + 1) * HALF],
                                                       start=True, stop=True)
                            ins.then_inc(scores_ready, 1)

                        def weigh_values(turn):
                            i, kc = turn // TT, turn % TT
                            if turn == 0:
                                pe.wait_ge(v_done, at * TT + TT)
                            if kc == 0 and i >= 2:
                                pe.wait_ge(o_copied, at * 2 * NG + i - 1)
                            pe.wait_ge(exp_done, at * N_ST + 2 * turn + 2)
                            for j in range(GH):
                                head = i // 2 * GH + j
                                ins = nc.tensor.matmul(ps[32 * j:32 * j + 32, 6 + i % 2], V[:, kc, head * VW:head * VW + 32],
                                                       prob[:, (2 * turn + j // 2) % 4, j % 2], start=(kc == 0), stop=(kc == TT - 1))
                            ins.then_inc(pv_done, 1)

                        for i in range(64):
                            maximum(0, i)
                        transpose_maxima(0)
                        for g in range(NG):
                            pe.wait_ge(neg_rows_loaded, at * 32 * NG + 32 * (g + 1))
                            left = 64 if g + 1 < NG else 0
                            for turn in range(2 * TT):
                                for pair in range(2):
                                    scores(g, turn // TT, turn % TT, pair)
                                if turn == 2 and g > 0:
                                    transpose_output(2 * g - 1)
                                if turn == 10:
                                    transpose_output(2 * g)
                                for _ in range(min(MAX_PER_TURN, left)):
                                    maximum(g + 1, 64 - left)
                                    left -= 1
                                if g > 0 or turn > 0:
                                    weigh_values(g * 2 * TT + turn - 1)
                            if g + 1 < NG:
                                transpose_maxima(g + 1)
                        weigh_values(N_PV - 1)
                        transpose_output(2 * NG - 1)

                    with pe.Else():
                        split_done(0, 0)
                        split_done(0, 1)
                        for t in range(TT):
                            if t >= 4:
                                pe.wait_ge(rows_copied, b * TT + t - 3)
                            for n in range(2):
                                ins = product(ps[:, 2 * (t % 4) + n, 0:3 * D // 2], acts(slice(t * P, (t + 1) * P)),
                                              weights(wq_hi, wq_lo, wq_x, slice(n * 3 * D // 2, (n + 1) * 3 * D // 2)))
                            ins.then_inc(v_ready, 1)

                    transpose_h(1, 0, 3)
                    transpose_h(1, 1, 3)
                    pe.wait_ge(wp_ready, it + 1)
                    for t in range(TT):
                        if t % HT == 0:
                            split_done(1, t // HT)
                        product(ps[:, (6, 7, 0, 1, 2, 3, 4, 5)[t], 0:D], acts(slice(t * P, (t + 1) * P)),
                                weights(wp_hi, wp_lo, wp_x, slice(0, D))).then_inc(proj_ready, 1)
                    transpose_h(2, 0, 4)
                    transpose_h(2, 1, 5)
                    for half in range(2):
                        split_done(2, half)
                        if half == 0:
                            split_done(2, 1)
                            pe.wait_ge(w1_ready, it + 1)
                            pe.wait_ge(w2_ready, it + 1)
                        for i in range(half * FC, (half + 1) * FC):
                            if i >= 2:
                                pe.wait_ge(gelu_done, it * 2 * FC + i - 1)
                            product(ps[:, 6 + i % 2], weights(w1_hi, w1_lo, w1_x, slice(i % FC * P, (i % FC + 1) * P)),
                                    acts(slice(half * HALF, (half + 1) * HALF))).then_inc(fc1_ready, 1)
                        for t in range(half * HT, (half + 1) * HT):
                            if t >= 6:
                                pe.wait_ge(x2_done, it * TT + t - 5)
                            cols = slice(t % HT * P, (t % HT + 1) * P)
                            bank = ps[:, t % 6, 0:D]
                            for c in range(FC):
                                if t % HT == 0:
                                    pe.wait_ge(hid_lo_done, it * 2 * FC + half * FC + c + 1)
                                nc.tensor.matmul(bank, hid_hi[:, c, cols], w2_hi[:, c], start=(c == 0), stop=False)
                                nc.tensor.matmul(bank, hid_lo[:, c, cols], w2_hi[:, c], start=False, stop=False)
                                nc.tensor.matmul(bank, hid_hi[:, c, cols], w2_lo[:, c], start=False, stop=False)
                            nc.tensor.matmul(bank, ones2[0:2], w2_b[0:2], start=False, stop=True).then_inc(fc2_ready, 1)


def kernel(**inputs):
    import numpy as np
    import concourse.bacc as bacc
    from concourse.bass_utils import run_bass_kernel_spmd

    a = {k: np.ascontiguousarray(v) for k, v in inputs.items()}
    f = np.float32
    zeros3, ones1, zeros1 = np.zeros(3 * D, f), np.ones(D, f), np.zeros(D, f)

    qkv_w = [a["L0_cond_W_qkv"],
             np.concatenate([a["L1_cond_wq"], a["L1_cond_wk"], a["L1_cond_wv"]], axis=1),
             a["L2_cond_qkv_w"], a["L3_cond_qkv_w"]]
    qkv_b = [a["L0_cond_b_qkv"], zeros3, a["L2_cond_qkv_b"], a["L3_cond_qkv_b"]]
    proj_w = [a["L0_cond_W_proj"], a["L1_cond_wo"], a["L2_cond_proj_w"], a["L3_cond_out_w"]]
    proj_b = [a["L0_cond_b_proj"], a["L1_cond_wo_b"], a["L2_cond_proj_b"], a["L3_cond_out_b"]]
    fc1_w = [a["L0_cond_W_fc1"], a["L1_cond_fc1_w"], a["L2_cond_fc1_w"], a["L3_cond_w1"]]
    fc1_b = [a["L0_cond_b_fc1"], a["L1_cond_fc1_b"], a["L2_cond_fc1_b"], a["L3_cond_b1"]]
    fc2_w = [a["L0_cond_W_fc2"], a["L1_cond_fc2_w"], a["L2_cond_fc2_w"], a["L3_cond_w2"]]
    fc2_b = [a["L0_cond_b_fc2"], a["L1_cond_fc2_b"], a["L2_cond_fc2_b"], a["L3_cond_b2"]]
    ada_w = [a["L0_cond_W_ada"], a["L1_cond_ada_w"], a["L2_cond_ada_w"], a["L3_cond_ada_w"]]
    ada_b = [a["L0_cond_b_ada"], a["L1_cond_ada_b"], a["L2_cond_ada_b"], a["L3_cond_ada_b"]]
    plain = np.stack([ones1, ones1, zeros1, zeros1])
    ln = [plain, np.stack([a["L1_cond_ln1_w"], a["L1_cond_ln2_w"], a["L1_cond_ln1_b"], a["L1_cond_ln2_b"]]),
          plain, plain]

    order = np.arange(D).reshape(NH, HD).T.reshape(-1)
    columns = np.concatenate([order, D + order, 2 * D + np.arange(D)])
    qkv_w = [w if l == CROSS else w[:, columns] for l, w in enumerate(qkv_w[:L])]
    qkv_b = [v if l == CROSS else v[columns] for l, v in enumerate(qkv_b[:L])]
    qkv_w, qkv_b = qkv_w + qkv_w[:1], qkv_b + qkv_b[:1]

    def main_rows(ws):
        return np.stack([w[:2 * P].reshape(2, P, -1) for w in ws])

    def last_rows(ws, bs):
        return np.stack([np.concatenate([w[2 * P:]] * 3 + [v[None]] * 2) for w, v in zip(ws, bs)])

    arrays = {
        "x_in": a["x"], "cond": a["cond_1152"].T.reshape(3, D // 3, B).transpose(1, 0, 2),
        "ada_w": np.stack(ada_w), "ada_b": np.stack(ada_b), "ln_rows": np.stack(ln),
        "w_qkv": main_rows(qkv_w), "w_qkv_x": last_rows(qkv_w, qkv_b),
        "w_proj": main_rows(proj_w), "w_proj_x": last_rows(proj_w, proj_b),
        "w_fc1": main_rows(fc1_w), "w_fc1_x": last_rows(fc1_w, fc1_b),
        "w_fc2": np.stack([w.reshape(FC, P, D) for w in fc2_w]),
        "b_fc2": np.stack([np.stack([v, v]) for v in fc2_b]),
    }
    nc = bacc.Bacc("TRN2", target_bir_lowering=False, num_devices=1)
    handles = []
    for name, value in arrays.items():
        arrays[name] = value = np.ascontiguousarray(value)
        handles.append(nc.dram_tensor(name, value.shape, mybir.dt.from_np(value.dtype), kind="ExternalInput").ap())
    out = nc.dram_tensor("out", (B, T, D), F32, kind="ExternalOutput").ap()
    build_program(nc, *handles, out)
    result = run_bass_kernel_spmd(nc, [arrays], core_ids=[0])
    return result.results[0]["out"]
```
